# Optimizing a Trainium2 kernel written in Bass

```python
import numpy as np
import jax
import jax.numpy as jnp

def _softmax(x, axis=-1):
    return jax.nn.softmax(x, axis=axis)

def _gelu(x):
    return jax.nn.gelu(x, approximate=True)

def _silu(x):
    return jax.nn.silu(x)

def _sigmoid(x):
    return jax.nn.sigmoid(x)

def _layernorm(x, axis=-1, eps=1e-05):
    m = jnp.mean(x, axis=axis, keepdims=True)
    v = jnp.var(x, axis=axis, keepdims=True)
    return (x - m) / jnp.sqrt(v + eps)

def _scatter_add(tgt, idx, src, axis=0):
    return tgt.at[idx].add(src)

def _segment_sum(src, seg, n):
    return jax.ops.segment_sum(src, seg, n)
kernel_name = 'mk_dlrm_tower_d1_rec_r8_8a80e6'

def setup_inputs(seed: int=0):
    np.random.seed(seed)
    _w = jnp.asarray

    def _rec_inputs():
        import jax
        import jax.numpy as jnp
        _tk = jax.random.key(seed)
        ids = jnp.stack([jax.random.randint(jax.random.fold_in(_tk, 200 + f), (2048,), 0, v, jnp.int32) for f, v in enumerate([12500, 125000, 1250, 12500, 1250, 12500, 12500, 1250, 1250, 1000, 12500, 12500, 1250, 1250, 12500, 1250, 12500, 1250, 1250, 1250, 1250, 1000, 1000, 1250, 1000, 1250])], axis=1)
        tbl_0 = 0.05 * jax.random.normal(jax.random.fold_in(_tk, 500 + 0), (12500, 128), jnp.float32)
        tbl_1 = 0.05 * jax.random.normal(jax.random.fold_in(_tk, 500 + 1), (125000, 128), jnp.float32)
        tbl_2 = 0.05 * jax.random.normal(jax.random.fold_in(_tk, 500 + 2), (1250, 128), jnp.float32)
        tbl_3 = 0.05 * jax.random.normal(jax.random.fold_in(_tk, 500 + 3), (12500, 128), jnp.float32)
        tbl_4 = 0.05 * jax.random.normal(jax.random.fold_in(_tk, 500 + 4), (1250, 128), jnp.float32)
        tbl_5 = 0.05 * jax.random.normal(jax.random.fold_in(_tk, 500 + 5), (12500, 128), jnp.float32)
        tbl_6 = 0.05 * jax.random.normal(jax.random.fold_in(_tk, 500 + 6), (12500, 128), jnp.float32)
        tbl_7 = 0.05 * jax.random.normal(jax.random.fold_in(_tk, 500 + 7), (1250, 128), jnp.float32)
        tbl_8 = 0.05 * jax.random.normal(jax.random.fold_in(_tk, 500 + 8), (1250, 128), jnp.float32)
        tbl_9 = 0.05 * jax.random.normal(jax.random.fold_in(_tk, 500 + 9), (1000, 128), jnp.float32)
        tbl_10 = 0.05 * jax.random.normal(jax.random.fold_in(_tk, 500 + 10), (12500, 128), jnp.float32)
        tbl_11 = 0.05 * jax.random.normal(jax.random.fold_in(_tk, 500 + 11), (12500, 128), jnp.float32)
        tbl_12 = 0.05 * jax.random.normal(jax.random.fold_in(_tk, 500 + 12), (1250, 128), jnp.float32)
        tbl_13 = 0.05 * jax.random.normal(jax.random.fold_in(_tk, 500 + 13), (1250, 128), jnp.float32)
        tbl_14 = 0.05 * jax.random.normal(jax.random.fold_in(_tk, 500 + 14), (12500, 128), jnp.float32)
        tbl_15 = 0.05 * jax.random.normal(jax.random.fold_in(_tk, 500 + 15), (1250, 128), jnp.float32)
        tbl_16 = 0.05 * jax.random.normal(jax.random.fold_in(_tk, 500 + 16), (12500, 128), jnp.float32)
        tbl_17 = 0.05 * jax.random.normal(jax.random.fold_in(_tk, 500 + 17), (1250, 128), jnp.float32)
        tbl_18 = 0.05 * jax.random.normal(jax.random.fold_in(_tk, 500 + 18), (1250, 128), jnp.float32)
        tbl_19 = 0.05 * jax.random.normal(jax.random.fold_in(_tk, 500 + 19), (1250, 128), jnp.float32)
        tbl_20 = 0.05 * jax.random.normal(jax.random.fold_in(_tk, 500 + 20), (1250, 128), jnp.float32)
        tbl_21 = 0.05 * jax.random.normal(jax.random.fold_in(_tk, 500 + 21), (1000, 128), jnp.float32)
        tbl_22 = 0.05 * jax.random.normal(jax.random.fold_in(_tk, 500 + 22), (1000, 128), jnp.float32)
        tbl_23 = 0.05 * jax.random.normal(jax.random.fold_in(_tk, 500 + 23), (1250, 128), jnp.float32)
        tbl_24 = 0.05 * jax.random.normal(jax.random.fold_in(_tk, 500 + 24), (1000, 128), jnp.float32)
        tbl_25 = 0.05 * jax.random.normal(jax.random.fold_in(_tk, 500 + 25), (1250, 128), jnp.float32)
        _rk = jax.random.fold_in(_tk, 7)
        r_bottom_output = -0.000520686 + 1.00062 * jax.random.normal(jax.random.fold_in(_rk, 101), (2048, 128), jnp.float32)
        W_top1 = 0.0456912 * jax.random.normal(jax.random.fold_in(_tk, 801), (479, 512), jnp.float32)
        W_top2 = 0.0441942 * jax.random.normal(jax.random.fold_in(_tk, 802), (512, 256), jnp.float32)
        W_top3 = 0.0625 * jax.random.normal(jax.random.fold_in(_tk, 803), (256, 1), jnp.float32)
        b_top1 = jnp.zeros((512,), jnp.float32)
        b_top2 = jnp.zeros((256,), jnp.float32)
        return (r_bottom_output, ids, tbl_0, tbl_1, tbl_2, tbl_3, tbl_4, tbl_5, tbl_6, tbl_7, tbl_8, tbl_9, tbl_10, tbl_11, tbl_12, tbl_13, tbl_14, tbl_15, tbl_16, tbl_17, tbl_18, tbl_19, tbl_20, tbl_21, tbl_22, tbl_23, tbl_24, tbl_25, W_top1, b_top1, W_top2, b_top2, W_top3)
    r_bottom_output, ids, tbl_0, tbl_1, tbl_2, tbl_3, tbl_4, tbl_5, tbl_6, tbl_7, tbl_8, tbl_9, tbl_10, tbl_11, tbl_12, tbl_13, tbl_14, tbl_15, tbl_16, tbl_17, tbl_18, tbl_19, tbl_20, tbl_21, tbl_22, tbl_23, tbl_24, tbl_25, W_top1, b_top1, W_top2, b_top2, W_top3 = _rec_inputs()

    def _L0_rec_setup():
        import jax, jax.numpy as jnp
        import numpy as np
        NUM_FEATURES = 27
        _TRIU_I, _TRIU_J = np.triu_indices(NUM_FEATURES, k=1)
        key = jax.random.key(seed)
        k1, k2 = jax.random.split(key)
        bottom_output = jax.random.normal(k1, (2048, 128), dtype=jnp.float32)
        embeddings = jax.random.normal(k2, (2048, 26, 128), dtype=jnp.float32)
        return {'bottom_output': bottom_output, 'embeddings': embeddings}
    _L0_rec_all = _L0_rec_setup()
    _L0_rec_in = {k: v for k, v in _L0_rec_all.items() if k in ()}
    del _L0_rec_all
    return {'r_bottom_output': r_bottom_output, 'ids': ids, 'tbl_0': tbl_0, 'tbl_1': tbl_1, 'tbl_2': tbl_2, 'tbl_3': tbl_3, 'tbl_4': tbl_4, 'tbl_5': tbl_5, 'tbl_6': tbl_6, 'tbl_7': tbl_7, 'tbl_8': tbl_8, 'tbl_9': tbl_9, 'tbl_10': tbl_10, 'tbl_11': tbl_11, 'tbl_12': tbl_12, 'tbl_13': tbl_13, 'tbl_14': tbl_14, 'tbl_15': tbl_15, 'tbl_16': tbl_16, 'tbl_17': tbl_17, 'tbl_18': tbl_18, 'tbl_19': tbl_19, 'tbl_20': tbl_20, 'tbl_21': tbl_21, 'tbl_22': tbl_22, 'tbl_23': tbl_23, 'tbl_24': tbl_24, 'tbl_25': tbl_25, 'W_top1': W_top1, 'b_top1': b_top1, 'W_top2': W_top2, 'b_top2': b_top2, 'W_top3': W_top3}

def reference(r_bottom_output, ids, tbl_0, tbl_1, tbl_2, tbl_3, tbl_4, tbl_5, tbl_6, tbl_7, tbl_8, tbl_9, tbl_10, tbl_11, tbl_12, tbl_13, tbl_14, tbl_15, tbl_16, tbl_17, tbl_18, tbl_19, tbl_20, tbl_21, tbl_22, tbl_23, tbl_24, tbl_25, W_top1, b_top1, W_top2, b_top2, W_top3):
    import jax
    import jax.numpy as jnp

    def _L0_rec_ref(bottom_output, embeddings):
        import jax, jax.numpy as jnp
        import numpy as np
        NUM_FEATURES = 27
        _TRIU_I, _TRIU_J = np.triu_indices(NUM_FEATURES, k=1)
        all_emb = jnp.concatenate([bottom_output[:, None, :], embeddings], axis=1)
        gram = jnp.einsum('bfd,bgd->bfg', all_emb, all_emb)
        return gram[:, _TRIU_I, _TRIU_J]
    e = jnp.stack([tbl_0[ids[:, 0]], tbl_1[ids[:, 1]], tbl_2[ids[:, 2]], tbl_3[ids[:, 3]], tbl_4[ids[:, 4]], tbl_5[ids[:, 5]], tbl_6[ids[:, 6]], tbl_7[ids[:, 7]], tbl_8[ids[:, 8]], tbl_9[ids[:, 9]], tbl_10[ids[:, 10]], tbl_11[ids[:, 11]], tbl_12[ids[:, 12]], tbl_13[ids[:, 13]], tbl_14[ids[:, 14]], tbl_15[ids[:, 15]], tbl_16[ids[:, 16]], tbl_17[ids[:, 17]], tbl_18[ids[:, 18]], tbl_19[ids[:, 19]], tbl_20[ids[:, 20]], tbl_21[ids[:, 21]], tbl_22[ids[:, 22]], tbl_23[ids[:, 23]], tbl_24[ids[:, 24]], tbl_25[ids[:, 25]]], axis=1)
    z = _L0_rec_ref(r_bottom_output, e)
    z = z.reshape(z.shape[0], -1)
    h = jnp.concatenate([z, r_bottom_output], axis=1)
    h = jnp.maximum(h @ W_top1 + b_top1, 0.0)
    h = jnp.maximum(h @ W_top2 + b_top2, 0.0)
    y = h @ W_top3
    return y

_drawn_inputs = setup_inputs


def setup_inputs(seed=0):
    import zlib

    import numpy as np

    out = dict(_drawn_inputs(seed))
    spreads = {'b_top1': (0.0, 0.1), 'b_top2': (0.0, 0.1)}
    factors = {}
    for name, (base, spread) in spreads.items():
        noise = np.random.default_rng([zlib.crc32(name.encode()), seed]).standard_normal(out[name].shape)
        drawn = base * np.exp(spread * noise) if base else spread * noise
        out[name] = jnp.asarray(drawn.astype(out[name].dtype))
    for name, factor in factors.items():
        out[name] = (out[name] * factor).astype(out[name].dtype)
    return out
```

```python
import concourse.bass as bass
from concourse import mybir
from contextlib import ExitStack
import numpy as np

P = 128
BATCH = 2048
TABLES = 26
NF = TABLES + 1
ROWS = 4
SBLK = ROWS * P
NSB = BATCH // SBLK
Q = 4
GPR = P // Q
NJ = NF - 1
H1, H2 = 512, 256
CHUNKS = [(1, 16), (16, 22), (22, 27)]
PAIRS = [sum(range(a, b)) for a, b in CHUNKS]
NPAIR = sum(PAIRS)
FGROUPS = [list(range(f, min(f + 4, NF))) for f in range(0, NF, 4)]


def pair_rows():
    row = {}
    for i in range(NF):
        for j in range(i + 1, NF):
            row[(i, j)] = len(row)
    return [row[(i, j)] for j in range(1, NF) for i in range(j)]


def dlrm_tower(nc, bottom, ids, tables, w1, b1, w2, b2, w3, out):
    F32 = mybir.dt.float32
    I32 = mybir.dt.int32
    U32 = mybir.dt.uint32
    ALU = mybir.AluOpType
    ACT = mybir.ActivationFunctionType

    with ExitStack() as ctx:
        def sb(name, shape, dt=F32):
            return ctx.enter_context(nc.sbuf_tensor(name, shape, dt))

        def psum(name, shape):
            return ctx.enter_context(nc.psum_tensor(name, shape, F32))

        def sem(name):
            return ctx.enter_context(nc.semaphore(name))

        idx_all = sb("idx_all", [P, NSB, ROWS, TABLES], U32)
        idx_cur = sb("idx_cur", [P, ROWS, TABLES], U32)
        rows = sb("rows", [P, ROWS, NF, P])
        embT = sb("embT", [P, 2, P, 32])
        botT = sb("botT", [P, SBLK])
        gram = sb("gram", [P, ROWS * GPR, NJ])
        zrow = sb("zrow", [P, NPAIR, Q])
        zT = sb("zT", [P, len(CHUNKS), SBLK])
        h1T = sb("h1T", [P, H1 // P, SBLK])
        h2T = sb("h2T", [P, H2 // P, SBLK])
        yrow = sb("yrow", [1, SBLK])
        w1_sb = sb("w1_sb", [P, len(CHUNKS) + 1, H1])
        w2_sb = sb("w2_sb", [P, H1 // P, H2])
        w3_sb = sb("w3_sb", [P, H2 // P])
        b1_sb = sb("b1_sb", [P, H1 // P])
        b2_sb = sb("b2_sb", [P, H2 // P])
        ident = sb("ident", [P, P])
        sel = sb("sel", [P, NJ, Q])

        featP = psum("featP", [P, 2, 4, P])
        gramP = psum("gramP", [P, 2, 2, 512])
        postP = psum("postP", [P, 2, 512])

        ids_in = sem("ids_in")
        weights_in = sem("weights_in")
        ident_zero = sem("ident_zero")
        ident_ready = sem("ident_ready")
        pad_ready = sem("pad_ready")
        sel_ready = sem("sel_ready")
        idx_ready = sem("idx_ready")
        rows_in = [[sem(f"rows_in_{r}_{g}") for g in range(len(FGROUPS))] for r in range(ROWS)]
        bottom_in = [sem(f"bottom_in_{r}") for r in range(ROWS)]
        rows_used = [sem(f"rows_used_{r}") for r in range(ROWS)]
        feat_full = [sem(f"feat_full_{b}") for b in range(2)]
        feat_free = [sem(f"feat_free_{b}") for b in range(2)]
        gram_full = [sem(f"gram_full_{b}") for b in range(2)]
        gram_free = [sem(f"gram_free_{b}") for b in range(2)]
        post_full = [sem(f"post_full_{b}") for b in range(2)]
        post_free = [sem(f"post_free_{b}") for b in range(2)]
        gathers_begun = sem("gathers_begun")
        y_stored = sem("y_stored")
        y_free = sem("y_free")

        bottom_t = bottom.rearrange("(t p) d -> t p d", p=P)
        NW = 5

        FEAT = [[sum(1 for g in range(len(FGROUPS)) if g % 2 == b) for b in range(2)]][0]
        UNITS = GPR // 8
        STEPS = ([("pairs", c) for c in range(3)] + [("pairsT", c) for c in range(3)]
                 + [("hidden1", o) for o in range(H1 // P)] + [("hidden2", o) for o in range(H2 // P)] + [("y", 0)])
        POST = [sum(1 for u in range(len(STEPS)) if u % 2 == b) for b in range(2)]

        def feat_count(s, r, g):
            return s * (ROWS * FEAT[g % 2]) + (r * FEAT[g % 2] + g // 2)

        def gram_count(s, r, u):
            return s * (ROWS * UNITS // 2) + (r * (UNITS // 2) + u // 2)

        def post_count(s, u):
            return s * POST[u % 2] + u // 2

        def step(name, c=0):
            return STEPS.index((name, c))

        block = ctx.enter_context(nc.Block())

        @block.sync
        def _(sp):
            sp.dma_start(idx_all[:], ids.rearrange("(s r p) f -> p s r f", p=P, r=ROWS)).then_inc(ids_in, 16)


            sp.sem_inc(y_free, 1)
            with sp.Fori(0, NSB) as s:
                for r in range(ROWS):
                    sp.wait_ge(rows_used[r], s + 1)
                    sp.dma_start(rows[:, r, 0, :],
                                 bottom_t[bass.ds(s * ROWS + r, 1), :, :].rearrange("t p d -> (t p) d")
                                 ).then_inc(bottom_in[r], 16)
                sp.wait_ge(post_free[step("y") % 2], post_count(s, step("y")) + 2)
                sp.dma_start(out[:, bass.ds(s * SBLK, SBLK)], yrow[0:1, :]).then_inc(y_stored, 16)
                sp.wait_ge(y_stored, (s + 1) * 16)
                sp.sem_inc(y_free, 1)
            sp.wait_ge(y_stored, 16 * NSB)

        @block.gpsimd
        def _(pool):
            nc.gpsimd.memset(ident[:], 0.0).then_inc(ident_zero, 1)
            pool.wait_ge(ident_zero, 1)
            nc.gpsimd.affine_select(out=ident[:], in_=ident[:], compare_op=ALU.not_equal, fill=1.0, base=0,
                                    pattern=[[-1, P]], channel_multiplier=1).then_inc(ident_ready, 1)
            pool.wait_ge(ids_in, 16)
            with pool.Fori(0, NSB) as s:
                for r in range(ROWS):
                    pool.wait_ge(rows_used[r], s + 1)
                    nc.gpsimd.tensor_copy(idx_cur[:, r, :],
                                          idx_all[:, bass.ds(s, 1), r, :].rearrange("p s f -> p (s f)")
                                          ).then_inc(idx_ready, 1)
                    pool.wait_ge(idx_ready, s * ROWS + (r + 1))
                    pool.sem_inc(gathers_begun, 1)
                    for t in range(TABLES):
                        f = t + 1
                        nc.gpsimd.indirect_dma_start(
                            rows[:, r, f, :], None, tables[t],
                            bass.IndirectOffsetOnAxis(ap=idx_cur[:, r, t:t + 1], axis=0),
                        ).then_inc(rows_in[r][f // 4], 16)

        def copy_features(eng, b, s, r):
            for g, feats in enumerate(FGROUPS):
                if g % 2 != b:
                    continue
                eng.wait_ge(feat_full[b], feat_count(s, r, g) + 1)
                n = len(feats)
                if g == 0:
                    nc.vector.tensor_copy(botT[:, r * P:(r + 1) * P], featP[:, b, 0, :])
                dst = embT[:, r % 2, :, feats[0]:feats[0] + n]
                src = featP[:, b, 0:n, :].rearrange("p f b -> p b f")
                if b == 0:
                    nc.vector.tensor_copy(dst, src).then_inc(feat_free[b], 1)
                else:
                    nc.scalar.copy(dst, src).then_inc(feat_free[b], 1)

        def copy_grams(eng, b, s, r):
            for u in range(UNITS):
                if u % 2 != b:
                    continue
                eng.wait_ge(gram_full[b], gram_count(s, r, u) + 1)
                for q in range(Q):
                    lo = r * GPR + 8 * u
                    dst = gram[32 * q:32 * q + 32, lo:lo + 8, :].rearrange("p (k g) j -> p k g j", k=2)
                    src = gramP[32 * q:32 * q + 32, b, :, 0:4 * Q * NJ].rearrange(
                        "p k (g c) -> p k g c", g=4)[:, :, :, q * NJ:(q + 1) * NJ]
                    if b == 0:
                        last = nc.vector.tensor_copy(dst, src)
                    else:
                        last = nc.scalar.copy(dst, src)
                last.then_inc(gram_free[b], 1)

        def copy_post(eng, b, s):
            for u, (kind, c) in enumerate(STEPS):
                if u % 2 != b:
                    continue
                eng.wait_ge(post_full[b], post_count(s, u) + 1)
                if kind == "pairs":
                    n, o = PAIRS[c], sum(PAIRS[:c])
                    dst = zrow[:, o:o + n, :].rearrange("p n q -> p (n q)")
                    src = postP[:, b, 0:n * Q]
                elif kind == "pairsT":
                    n = PAIRS[c]
                    dst = zT[0:n, c, :].rearrange("p (g q) -> p g q", q=Q)
                    src = postP[0:n, b, :].rearrange("p (q g) -> p g q", q=Q)
                elif kind == "y":
                    dst, src = yrow[0:1, :], postP[0:1, b, :]
                    eng.wait_ge(y_free, s + 1)
                else:
                    dst = (h1T if kind == "hidden1" else h2T)[:, c, :]
                    src = postP[:, b, :]
                if kind in ("hidden1", "hidden2"):
                    bias = (b1_sb if kind == "hidden1" else b2_sb)[:, c:c + 1]
                    if b == 0:
                        op = nc.vector.tensor_scalar(dst, src, bias, 0.0, ALU.add, ALU.max)
                    else:
                        op = nc.scalar.activation(dst, src, ACT.Relu, bias=bias)
                elif b == 0:
                    op = nc.vector.tensor_copy(dst, src)
                else:
                    op = nc.scalar.copy(dst, src)
                op.then_inc(post_free[b], 1)

        @block.vector
        def _(dve):
            nc.vector.memset(embT[:, :, :, NF:32], 0.0).then_inc(pad_ready, 1)
            dve.wait_ge(ident_ready, 1)
            nc.vector.tensor_copy(sel[:], ident[:].rearrange("p (q i) -> p i q", q=Q)[:, 0:NJ, :]).then_inc(sel_ready, 1)
            dve.wait_ge(weights_in, 16 * 8)
            for free in (feat_free[0], gram_free[0], post_free[0]):
                dve.sem_inc(free, 1)
            with dve.Fori(0, NSB) as s:
                for r in range(ROWS):
                    copy_features(dve, 0, s, r)
                    copy_grams(dve, 0, s, r)
                copy_post(dve, 0, s)

        @block.scalar
        def _(act):
            n = 0
            w1p = w1[0:NPAIR, :]
            for c, k in enumerate(PAIRS):
                act.dma_start(w1_sb[0:k, c, :], w1p[n:n + k, :]).then_inc(weights_in, 16)
                n += k
            act.dma_start(w1_sb[:, 3, :], w1[NPAIR:NPAIR + P, :]).then_inc(weights_in, 16)
            act.dma_start(w2_sb[:], w2.rearrange("(c p) n -> p c n", p=P)).then_inc(weights_in, 16)
            act.dma_start(w3_sb[:], w3).then_inc(weights_in, 16)
            act.dma_start(b1_sb[:], b1).then_inc(weights_in, 16)
            act.dma_start(b2_sb[:], b2).then_inc(weights_in, 16)
            act.wait_ge(weights_in, 16 * 8)
            for free in (feat_free[1], gram_free[1], post_free[1]):
                act.sem_inc(free, 1)
            with act.Fori(0, NSB) as s:
                for r in range(ROWS):
                    copy_features(act, 1, s, r)
                    copy_grams(act, 1, s, r)
                copy_post(act, 1, s)

        @block.tensor
        def _(pe):
            for r in range(ROWS):
                pe.sem_inc(rows_used[r], 1)
            pe.wait_ge(ident_ready, 1)
            pe.wait_ge(pad_ready, 1)
            pe.wait_ge(sel_ready, 1)
            pe.wait_ge(weights_in, 16 * 8)

            def post_begin(s, u):
                pe.wait_ge(post_free[u % 2], post_count(s, u) + 1)
                return postP[:, u % 2, :]

            def copied(s, u):
                pe.wait_ge(post_free[u % 2], post_count(s, u) + 2)

            with pe.Fori(0, NSB) as s:
                for r in range(ROWS):
                    for g, feats in enumerate(FGROUPS):
                        b = g % 2
                        if g == 0:
                            pe.wait_ge(bottom_in[r], (s + 1) * 16)
                        gathered = sum(1 for f in feats if f > 0)
                        pe.wait_ge(rows_in[r][g], (s + 1) * (16 * gathered))
                        pe.wait_ge(feat_free[b], feat_count(s, r, g) + 1)
                        for k, f in enumerate(feats):
                            last = nc.tensor.transpose(featP[:, b, k, :], rows[:, r, f, :], ident[:])
                        last.then_inc(feat_full[b], 1)
                    for g in (len(FGROUPS) - 2, len(FGROUPS) - 1):
                        pe.wait_ge(feat_free[g % 2], feat_count(s, r, g) + 2)
                    for u in range(UNITS):
                        b = u % 2
                        pe.wait_ge(gram_free[b], gram_count(s, r, u) + 1)
                        for k in range(8):
                            n = (8 * u + k) * Q
                            lhs = embT[:, r % 2, n:n + Q, :].rearrange("p b f -> p (b f)")
                            last = nc.tensor.matmul(gramP[:, b, k // 4, (k % 4) * Q * NJ:(k % 4 + 1) * Q * NJ],
                                                    lhs, embT[:, r % 2, n:n + Q, 1:NF], start=True, stop=True)
                            if u == k == 0:
                                last.then_inc(rows_used[r], 1)
                        last.then_inc(gram_full[b], 1)
                for b in range(2):
                    pe.wait_ge(gram_free[b], gram_count(s, ROWS - 1, UNITS - 2 + b) + 2)
                for c, (j0, j1) in enumerate(CHUNKS):
                    bank = post_begin(s, step("pairs", c))
                    at = 0
                    for j in range(j0, j1):
                        last = nc.tensor.matmul(bank[:, at:at + Q * j], gram[:, :, j - 1],
                                                sel[:, 0:j, :].rearrange("p i q -> p (i q)"), start=True, stop=True)
                        at += Q * j
                    last.then_inc(post_full[step("pairs", c) % 2], 1)
                for c, n in enumerate(PAIRS):
                    copied(s, step("pairs", c))
                    bank = post_begin(s, step("pairsT", c))
                    o = sum(PAIRS[:c])
                    for q in range(Q):
                        last = nc.tensor.transpose(bank[0:n, q * P:(q + 1) * P], zrow[:, o:o + n, q], ident[:])
                    last.then_inc(post_full[step("pairsT", c) % 2], 1)
                for c in range(3):
                    copied(s, step("pairsT", c))
                for o in range(H1 // P):
                    bank = post_begin(s, step("hidden1", o))
                    col = slice(o * P, (o + 1) * P)
                    nc.tensor.matmul(bank, w1_sb[:, 3, col], botT[:], start=True, stop=False)
                    for c, n in enumerate(PAIRS):
                        last = nc.tensor.matmul(bank, w1_sb[0:n, c, col], zT[0:n, c, :], start=False, stop=c == 2)
                    last.then_inc(post_full[step("hidden1", o) % 2], 1)
                for o in range(H1 // P):
                    copied(s, step("hidden1", o))
                for o in range(H2 // P):
                    bank = post_begin(s, step("hidden2", o))
                    for k in range(H1 // P):
                        last = nc.tensor.matmul(bank, w2_sb[:, k, o * P:(o + 1) * P], h1T[:, k, :],
                                                start=k == 0, stop=k == H1 // P - 1)
                    last.then_inc(post_full[step("hidden2", o) % 2], 1)
                for o in range(H2 // P):
                    copied(s, step("hidden2", o))
                bank = post_begin(s, step("y"))
                for k in range(H2 // P):
                    last = nc.tensor.matmul(bank[0:1, :], w3_sb[:, k:k + 1], h2T[:, k, :], start=k == 0, stop=k == 1)
                last.then_inc(post_full[step("y") % 2], 1)


def kernel(**inputs):
    import concourse.bacc as _bacc
    from concourse import mybir as _mybir
    from concourse.bass_utils import run_bass_kernel_spmd as _run

    nc = _bacc.Bacc("TRN2", target_bir_lowering=False, num_devices=1)
    arrays = {}

    def dram(name, a):
        a = np.ascontiguousarray(a)
        arrays[name] = a
        return nc.dram_tensor(name, a.shape, _mybir.dt.from_np(a.dtype), kind="ExternalInput").ap()

    w1 = np.asarray(inputs["W_top1"])
    order = pair_rows() + list(range(NPAIR, w1.shape[0]))
    bottom = dram("bottom", inputs["r_bottom_output"])
    ids = dram("ids", np.ascontiguousarray(inputs["ids"]).view(np.uint32))
    tables = [dram(f"table_{t}", inputs[f"tbl_{t}"]) for t in range(TABLES)]

    def columns(name):
        return np.asarray(inputs[name]).reshape(-1, P).T

    w = [dram("w1", w1[order]), dram("b1", columns("b_top1")), dram("w2", inputs["W_top2"]),
         dram("b2", columns("b_top2")), dram("w3", columns("W_top3"))]
    out = nc.dram_tensor("y", (1, BATCH), _mybir.dt.float32, kind="ExternalOutput").ap()
    dlrm_tower(nc, bottom, ids, tables, *w, out)
    r = _run(nc, [arrays], core_ids=[0])
    return r.results[0]["y"].reshape(BATCH, 1)
```

```python
import concourse.bass as bass
from concourse import mybir
from contextlib import ExitStack
import numpy as np

P = 128
BATCH = 2048
TABLES = 26
NF = TABLES + 1
TABLE_ROWS = [12500, 125000, 1250, 12500, 1250, 12500, 12500, 1250, 1250, 1000, 12500, 12500, 1250, 1250,
              12500, 1250, 12500, 1250, 1250, 1250, 1250, 1000, 1000, 1250, 1000, 1250]
HOT = [9, 21, 22, 24, 2, 4, 7]
COLD = [t for t in range(TABLES) if t not in HOT]
HP = 125
CUT = [TABLE_ROWS[t] // HP for t in HOT]
PARTS = 2
NHOT, NCOLD = len(HOT), len(COLD)
NR = NCOLD + 1
ORDER = [0] + [t + 1 for t in COLD] + [t + 1 for t in HOT]

ROWS = 4
SBLK = ROWS * P
HALF = SBLK // 2
NSB = BATCH // SBLK
Q = 4
GPR = P // Q
GU = 4
UNITS = GPR // GU
NJ = NF - 1
H1, H2 = 512, 256
CHUNKS = [(1, 16), (16, 22), (22, 27)]
PAIRS = [sum(range(a, b)) for a, b in CHUNKS]
NPAIR = sum(PAIRS)
JGROUPS = [list(range(j, min(j + 4, NF))) for j in range(1, NF, 4)]
FGROUPS = [list(range(f, min(f + 4, NR))) for f in range(0, NR, 4)]


def pair_rows():
    row = {}
    for i in range(NF):
        for j in range(i + 1, NF):
            row[(i, j)] = len(row)
    return [row[tuple(sorted((ORDER[i], ORDER[j])))] for j in range(1, NF) for i in range(j)]


def dlrm_tower(nc, bottom, ids, hot_ids, tables, w1, b1, w2, b2, w3, out):
    F32 = mybir.dt.float32
    F32R = mybir.dt.float32r
    I32 = mybir.dt.int32
    U32 = mybir.dt.uint32
    ALU = mybir.AluOpType
    ACT = mybir.ActivationFunctionType

    with ExitStack() as ctx:
        def sb(name, shape, dt=F32):
            return ctx.enter_context(nc.sbuf_tensor(name, shape, dt))

        def psum(name, shape):
            return ctx.enter_context(nc.psum_tensor(name, shape, F32))

        def sem(name):
            return ctx.enter_context(nc.semaphore(name))

        idx_all = sb("idx_all", [P, NSB, ROWS, NCOLD], U32)
        idx_cur = sb("idx_cur", [P, ROWS, NCOLD], U32)
        rows = sb("rows", [P, ROWS, NR, P])
        hot_hi = [sb(f"hot_hi_{n}", [HP, CUT[n], P], F32R) for n in range(NHOT)]
        hot_lo = [sb(f"hot_lo_{n}", [HP, CUT[n], P], F32R) for n in range(NHOT)]
        hot_idf = sb("hot_idf", [P, NSB, HALF], F32R)
        onehot = sb("onehot", [HP, 2, PARTS, max(CUT) // PARTS, HALF], F32R)
        rowid = {c: sb(f"rowid_{c}", [HP, c]) for c in sorted(set(CUT))}
        embT = sb("embT", [P, 2, P, 32])
        botT = sb("botT", [P, SBLK])
        gram = sb("gram", [P, ROWS * GPR, NJ])
        wide = sb("wide", [P, H1 // P * SBLK])
        zT = sb("zT", [P, len(CHUNKS), SBLK])
        zrow = wide[:, 0:NPAIR * Q].rearrange("p (n q) -> p n q", q=Q)
        h1T = wide[:].rearrange("p (o b) -> p o b", o=H1 // P)
        h2T = zT[:, 0:H2 // P, :]
        yrow = sb("yrow", [1, SBLK])
        w1_sb = sb("w1_sb", [P, len(CHUNKS) + 1, H1])
        w2_sb = sb("w2_sb", [P, H1 // P, H2])
        w3_sb = sb("w3_sb", [P, H2 // P])
        b1_sb = sb("b1_sb", [P, H1 // P])
        b2_sb = sb("b2_sb", [P, H2 // P])
        ident = sb("ident", [P, P])
        identR = sb("identR", [P, P], F32R)
        perm = sb("perm", [P, 32, Q])
        gram_flat = gram[:].rearrange("p g j -> p (g j)")
        narrow, broad = 8 * P, 10 * P
        staging = [gram_flat[0:HP, 0:narrow], gram_flat[0:HP, narrow:2 * narrow], gram_flat[0:HP, 2 * narrow:3 * narrow],
                   wide[0:HP, 0:narrow],
                   gram_flat[0:HP, 0:broad], gram_flat[0:HP, broad:2 * broad], wide[0:HP, 0:broad]]
        stage_after = [0, 0, 0, 0, 2, 3, 4]
        hot_int = zT[:].rearrange("p c b -> p (c b)").bitcast(I32)[0:2 * NHOT, 0:NSB * HALF]

        featP = psum("featP", [P, 2, 4, P])
        gramP = psum("gramP", [P, 2, 512])
        idsP = psum("idsP", [P, 2, 2, HALF])
        postP = psum("postP", [P, 2, 512])

        ids_in = sem("ids_in")
        hot_ids_in = sem("hot_ids_in")
        table_in = [sem(f"table_in_{n}") for n in range(NHOT)]
        weights_in = sem("weights_in")
        hi_ready = sem("hi_ready")
        lo_ready = sem("lo_ready")
        ident_zero = sem("ident_zero")
        ident_ready = sem("ident_ready")
        rowid_ready = sem("rowid_ready")
        idf_zero = sem("idf_zero")
        consts_ready = sem("consts_ready")
        idx_ready = sem("idx_ready")
        gathers_begun = sem("gathers_begun")
        rows_in = [[sem(f"rows_in_{r}_{g}") for g in range(len(FGROUPS))] for r in range(ROWS)]
        bottom_in = [sem(f"bottom_in_{r}") for r in range(ROWS)]
        rows_used = [sem(f"rows_used_{r}") for r in range(ROWS)]
        onehot_ready = sem("onehot_ready")
        onehot_used = sem("onehot_used")
        ids_full = [sem(f"ids_full_{b}") for b in range(2)]
        feat_full = [sem(f"feat_full_{b}") for b in range(2)]
        feat_free = [sem(f"feat_free_{b}") for b in range(2)]
        gram_full = [sem(f"gram_full_{b}") for b in range(2)]
        gram_free = [sem(f"gram_free_{b}") for b in range(2)]
        post_full = [sem(f"post_full_{b}") for b in range(2)]
        post_free = [sem(f"post_free_{b}") for b in range(2)]
        y_stored = sem("y_stored")
        y_free = sem("y_free")

        bottom_t = bottom.rearrange("(t p) d -> t p d", p=P)
        NWEIGHTS = 8

        def order(h, more):
            first, second = 2 * h, 2 * h + 1
            groups = range(len(FGROUPS))
            uses = []
            for n in range(NHOT):
                uses.append(("hot", h, n))
                if n >= 1 and n - 1 in groups:
                    uses.append(("rows", first, n - 1))
            if more:
                uses.append(("rows", second, 0))
            for u in range(UNITS):
                uses.append(("gram", first, u))
                if more and u >= 2 and u - 1 in groups:
                    uses.append(("rows", second, u - 1))
            if not more:
                uses += [("rows", second, g) for g in groups]
            return uses + [("gram", second, u) for u in range(UNITS)]

        FEAT = [x for h in range(2) for x in order(h, True) if x[0] != "gram"]
        HOT_OF = [[("hot", h, n) for n in range(NHOT)] for h in range(2)]
        GRAM = [("gram", r, u) for r in range(ROWS) for u in range(UNITS)]
        IDS = [(h, v) for h in range(2) for v in range((NHOT + 1) // 2)]
        POST = ([("pairs", c) for c in range(len(JGROUPS))] + [("pairsT", c) for c in range(3)]
                + [("hidden1", o) for o in range(H1 // P)] + [("hidden2", o) for o in range(H2 // P)] + [("y", 0)])

        def used(ring, s, item):
            u = ring.index(item)
            return u % 2, s * len(ring[u % 2::2]) + u // 2

        SB_BATCHES = 2 * NHOT * PARTS

        def batch_at(h, n, k):
            return (h * NHOT + n) * PARTS + k

        def onehot_place(h, n):
            return (h * NHOT + n) % 2

        block = ctx.enter_context(nc.Block())

        @block.sync
        def _(sp):
            sp.dma_start(idx_all[:], ids.rearrange("(s r p) f -> p s r f", p=P, r=ROWS)).then_inc(ids_in, 16)
            sp.dma_start(hot_int, hot_ids).then_inc(hot_ids_in, 16)
            for r in range(ROWS):
                sp.dma_start(rows[:, r, 0, :], bottom_t[r]).then_inc(bottom_in[r], 16)
            for n, t in enumerate(HOT):
                if stage_after[n]:
                    sp.wait_ge(lo_ready, stage_after[n])
                sp.dma_start(staging[n], tables[t].rearrange("(p c) d -> p (c d)", p=HP)).then_inc(table_in[n], 16)
            n = 0
            for c, k in enumerate(PAIRS):
                sp.dma_start(w1_sb[0:k, c, :], w1[n:n + k, :]).then_inc(weights_in, 16)
                n += k
            sp.dma_start(w1_sb[:, 3, :], w1[NPAIR:NPAIR + P, :]).then_inc(weights_in, 16)
            sp.dma_start(w2_sb[:], w2.rearrange("(c p) n -> p c n", p=P)).then_inc(weights_in, 16)
            for dst, src in ((w3_sb, w3), (b1_sb, b1), (b2_sb, b2)):
                sp.dma_start(dst[:], src).then_inc(weights_in, 16)

            def store(s):
                b, n = used(POST, s, ("y", 0))
                sp.wait_ge(post_free[b], n + 2)
                where = out[:, bass.ds(s * SBLK, SBLK)]
                sp.dma_start(where, yrow[0:1, :]).then_inc(y_stored, 16)
                sp.wait_ge(y_stored, (s + 1) * 16)
                sp.sem_inc(y_free, 1)

            sp.sem_inc(y_free, 1)
            with sp.Fori(0, NSB - 1) as s:
                for r in range(ROWS):
                    sp.wait_ge(rows_used[r], s + 2)
                    sp.dma_start(rows[:, r, 0, :],
                                 bottom_t[bass.ds((s + 1) * ROWS + r, 1), :, :].rearrange("t p d -> (t p) d")
                                 ).then_inc(bottom_in[r], 16)
                store(s)
            store(NSB - 1)
            sp.wait_ge(y_stored, 16 * NSB)

        @block.gpsimd
        def _(pool):
            nc.gpsimd.memset(ident[:], 0.0).then_inc(ident_zero, 1)
            pool.wait_ge(ident_zero, 1)
            nc.gpsimd.affine_select(out=ident[:], in_=ident[:], compare_op=ALU.not_equal, fill=1.0, base=0,
                                    pattern=[[-1, P]], channel_multiplier=1).then_inc(ident_ready, 1)
            for c in rowid:
                nc.gpsimd.iota(rowid[c][:], [[1, c]], base=0, channel_multiplier=c,
                               allow_small_or_imprecise_dtypes=True).then_inc(rowid_ready, 1)
            pool.wait_ge(ids_in, 16)
            with pool.Fori(0, NSB) as s:
                for r in range(ROWS):
                    pool.wait_ge(rows_used[r], s + 1)
                    nc.gpsimd.tensor_copy(idx_cur[:, r, :],
                                          idx_all[:, bass.ds(s, 1), r, :].rearrange("p s f -> p (s f)")
                                          ).then_inc(idx_ready, 1)
                    pool.wait_ge(idx_ready, s * ROWS + (r + 1))
                    pool.sem_inc(gathers_begun, 1)
                    for k, t in enumerate(COLD):
                        nc.gpsimd.indirect_dma_start(
                            rows[:, r, k + 1, :], None, tables[t],
                            bass.IndirectOffsetOnAxis(ap=idx_cur[:, r, k:k + 1], axis=0),
                        ).then_inc(rows_in[r][(k + 1) // 4], 16)

        def copy(eng, dst, src):
            return nc.vector.tensor_copy(dst, src) if eng is nc.vector else nc.scalar.copy(dst, src)

        def copy_hot(wait, eng, s, h, n):
            b, k = used(FEAT, s, ("hot", h, n))
            wait(feat_full[b], k + 1)
            for tile in range(2):
                last = copy(eng, embT[:, tile, :, NR + n], featP[:, b, tile, :])
            last.then_inc(feat_free[b], 1)

        def copy_rows(wait, eng, s, r, g):
            b, k = used(FEAT, s, ("rows", r, g))
            wait(feat_full[b], k + 1)
            feats = FGROUPS[g]
            if g == 0:
                copy(eng, botT[:, r * P:(r + 1) * P], featP[:, b, 0, :])
            copy(eng, embT[:, r % 2, :, feats[0]:feats[-1] + 1],
                 featP[:, b, 0:len(feats), :].rearrange("p f b -> p b f")).then_inc(feat_free[b], 1)

        def copy_gram(wait, eng, s, r, u):
            b, k = used(GRAM, s, ("gram", r, u))
            wait(gram_full[b], k + 1)
            lo = r * GPR + GU * u
            for q in range(Q):
                last = copy(eng, gram[32 * q:32 * q + 32, lo:lo + GU, :],
                            gramP[32 * q:32 * q + 32, b, 0:GU * Q * NJ].rearrange(
                                "p (g c) -> p g c", g=GU)[:, :, q * NJ:(q + 1) * NJ])
            last.then_inc(gram_free[b], 1)

        def copy_post(wait, eng, s, kind, c):
            b, k = used(POST, s, (kind, c))
            wait(post_full[b], k + 1)
            if kind == "pairs":
                for m, j in enumerate(JGROUPS[c]):
                    at = j * (j - 1) // 2
                    op = copy(eng, zrow[:, at:at + j, :].rearrange("p n q -> p (n q)"),
                              postP[:, b, m * P:m * P + Q * j])
            elif kind == "pairsT":
                n = PAIRS[c]
                op = copy(eng, zT[0:n, c, :].rearrange("p (g q) -> p g q", q=Q),
                          postP[0:n, b, :].rearrange("p (q g) -> p g q", q=Q))
            elif kind == "y":
                wait(y_free, s + 1)
                op = copy(eng, yrow[0:1, :], postP[0:1, b, :])
            else:
                dst = (h1T if kind == "hidden1" else h2T)[:, c, :]
                wait(weights_in, 16 * NWEIGHTS)
                bias = (b1_sb if kind == "hidden1" else b2_sb)[:, c:c + 1]
                if eng is nc.vector:
                    op = nc.vector.tensor_scalar(dst, postP[:, b, :], bias, 0.0, ALU.add, ALU.max)
                else:
                    op = nc.scalar.activation(dst, postP[:, b, :], ACT.Relu, bias=bias)
            op.then_inc(post_free[b], 1)

        def on_vector(item):
            return POST.index(item) % 2 == 0

        @block.vector
        def _(dve):
            wait = dve.wait_ge
            nc.vector.memset(embT[:, :, :, NF:32], 0.0).then_inc(consts_ready, 1)
            nc.vector.memset(hot_idf[:].bitcast(F32), 0.0).then_inc(idf_zero, 1)
            wait(ident_ready, 1)
            nc.vector.tensor_copy(perm[:], ident[:].rearrange("p (q i) -> p i q", q=Q)).then_inc(consts_ready, 1)
            nc.vector.tensor_copy(identR[:], ident[:]).then_inc(consts_ready, 1)
            wait(hot_ids_in, 16)
            wait(idf_zero, 1)
            nc.vector.tensor_copy(hot_idf[0:2 * NHOT, :, :].rearrange("p s b -> p (s b)"),
                                  hot_int).then_inc(consts_ready, 1)
            wait(rowid_ready, len(rowid))

            def split(n):
                wait(hi_ready, n + 1)
                nc.vector.tensor_tensor(hot_lo[n][:].rearrange("p c d -> p (c d)"), staging[n],
                                        hot_hi[n][:].bitcast(F32).rearrange("p c d -> p (c d)"),
                                        ALU.subtract).then_inc(lo_ready, 1)

            def make_onehot(s, h, n):
                b, k = used(IDS, s, (h, n // 2))
                if n % 2 == 0:
                    wait(ids_full[b], k + 1)
                m = CUT[n] // PARTS
                for k in range(PARTS):
                    wait(onehot_used, s * SB_BATCHES + (SB_BATCHES + batch_at(h, n, k) - 2 * PARTS + 1))
                    nc.vector.tensor_tensor(
                        onehot[:, onehot_place(h, n), k, 0:m, :],
                        idsP[0:HP, b, n % 2, :].unsqueeze(1).to_broadcast([HP, m, HALF]),
                        rowid[CUT[n]][:, k * m:(k + 1) * m].unsqueeze(2).to_broadcast([HP, m, HALF]),
                        ALU.is_equal).then_inc(onehot_ready, 1)

            def superblock(s, more):
                for h in range(2):
                    for n in range(2, NHOT):
                        make_onehot(s, h, n)
                    if h == 0 or more:
                        for n in range(2):
                            make_onehot(*((s, 1) if h == 0 else (s + 1, 0)), n)
                for item in POST:
                    if on_vector(item):
                        copy_post(wait, nc.vector, s, *item)

            for free in (feat_free, gram_free, post_free):
                for b in range(2):
                    dve.sem_inc(free[b], 1)
            dve.sem_inc(onehot_used, SB_BATCHES)
            for n in range(NHOT):
                split(n)
                if n < 2:
                    make_onehot(0, 0, n)
            with dve.Fori(0, NSB - 1) as s:
                superblock(s, True)
            superblock(NSB - 1, False)

        @block.scalar
        def _(act):
            wait = act.wait_ge
            for n in range(NHOT):
                wait(table_in[n], 16)
                nc.scalar.copy(hot_hi[n][:].rearrange("p c d -> p (c d)"), staging[n]).then_inc(hi_ready, 1)

            def superblock(s, more):
                for h in range(2):
                    for kind, x, y in order(h, h == 0 or more):
                        copy_of = {"hot": copy_hot, "rows": copy_rows, "gram": copy_gram}[kind]
                        copy_of(wait, nc.scalar, s, x, y)
                for item in POST:
                    if not on_vector(item):
                        copy_post(wait, nc.scalar, s, *item)

            with act.Fori(0, NSB - 1) as s:
                superblock(s, True)
            superblock(NSB - 1, False)

        @block.tensor
        def _(pe):
            wait = pe.wait_ge
            for r in range(ROWS):
                pe.sem_inc(rows_used[r], 1)
            wait(ident_ready, 1)
            wait(consts_ready, 4)

            def spread_ids(s, h, v):
                b, k = used(IDS, s, (h, v))
                for n in range(2 * v, min(2 * v + 2, NHOT)):
                    row = 2 * n + h
                    last = nc.tensor.matmul(idsP[:, b, n % 2, :], identR[:, row:row + 1].to_broadcast([P, P]),
                                            hot_idf[:, bass.ds(s, 1), :].rearrange("p s b -> p (s b)"),
                                            start=True, stop=True)
                last.then_inc(ids_full[b], 1)

            def pick_hot(s, h, n):
                b, k = used(FEAT, s, ("hot", h, n))
                wait(feat_free[b], k + 1)
                acc = featP[:, b, 0:2, :].rearrange("p t b -> p (t b)")
                m = CUT[n] // PARTS
                for k in range(PARTS):
                    wait(onehot_ready, s * SB_BATCHES + (batch_at(h, n, k) + 1))
                    for c in range(m):
                        columns = onehot[:, onehot_place(h, n), k, c, :]
                        first, end = k == c == 0, k == PARTS - 1 and c == m - 1
                        hi = nc.tensor.matmul(acc, hot_hi[n][:, k * m + c, :], columns, start=first, stop=False)
                        lo = nc.tensor.matmul(acc, hot_lo[n][:, k * m + c, :], columns, start=False, stop=end)
                        if n == 1 and first:
                            hi.then_inc(onehot_used, 1)
                    if k < PARTS - 1:
                        lo.then_inc(onehot_used, 1)
                lo.then_inc(feat_full[b], 1)

            def transpose_rows(s, r, g):
                b, k = used(FEAT, s, ("rows", r, g))
                feats = FGROUPS[g]
                if g == 0:
                    wait(bottom_in[r], (s + 1) * 16)
                wait(rows_in[r][g], (s + 1) * (16 * sum(1 for f in feats if f > 0)))
                wait(feat_free[b], k + 1)
                for m, f in enumerate(feats):
                    last = nc.tensor.transpose(featP[:, b, m, :], rows[:, r, f, :], ident[:])
                    if m == 0 and (r % 2 == 0 or g == 0):
                        last.then_inc(onehot_used, 1)
                last.then_inc(feat_full[b], 1)

            def gram_unit(s, r, u):
                b, k = used(GRAM, s, ("gram", r, u))
                if u == 0:
                    for side in range(2):
                        its = [x for x in FEAT[side::2] if x in HOT_OF[r // 2] or x[:2] == ("rows", r)]
                        fb, fk = used(FEAT, s, its[-1])
                        wait(feat_free[fb], fk + 2)
                wait(gram_free[b], k + 1)
                for m in range(GU):
                    at = (GU * u + m) * Q
                    last = nc.tensor.matmul(gramP[:, b, m * Q * NJ:(m + 1) * Q * NJ],
                                            embT[:, r % 2, at:at + Q, :].rearrange("p b f -> p (b f)"),
                                            embT[:, r % 2, at:at + Q, 1:NF], start=True, stop=True)
                    if u == m == 0:
                        last.then_inc(rows_used[r], 1)
                last.then_inc(gram_full[b], 1)

            def begin(s, *item):
                b, k = used(POST, s, item)
                wait(post_free[b], k + 1)
                return b

            def copied(s, *item):
                b, k = used(POST, s, item)
                wait(post_free[b], k + 2)

            def tower(s):
                for item in GRAM[-2:]:
                    b, k = used(GRAM, s, item)
                    wait(gram_free[b], k + 2)
                for c, js in enumerate(JGROUPS):
                    b = begin(s, "pairs", c)
                    for m, j in enumerate(js):
                        last = nc.tensor.transpose(postP[:, b, m * P:(m + 1) * P], gram[:, :, j - 1],
                                                   perm[:].rearrange("p i q -> p (i q)"))
                    last.then_inc(post_full[b], 1)
                for item in (("pairs", len(JGROUPS) - 2), ("pairs", len(JGROUPS) - 1)):
                    copied(s, *item)
                wait(weights_in, 16 * NWEIGHTS)
                for c, n in enumerate(PAIRS):
                    b = begin(s, "pairsT", c)
                    o = sum(PAIRS[:c])
                    for q in range(Q):
                        last = nc.tensor.transpose(postP[0:n, b, q * P:(q + 1) * P], zrow[:, o:o + n, q], ident[:])
                    last.then_inc(post_full[b], 1)
                for o in range(H1 // P):
                    b = begin(s, "hidden1", o)
                    col = slice(o * P, (o + 1) * P)
                    nc.tensor.matmul(postP[:, b, :], w1_sb[:, 3, col], botT[:], start=True, stop=False)
                    for c, n in enumerate(PAIRS):
                        if o == 0:
                            copied(s, "pairsT", c)
                        last = nc.tensor.matmul(postP[:, b, :], w1_sb[0:n, c, col], zT[0:n, c, :],
                                                start=False, stop=c == 2)
                    last.then_inc(post_full[b], 1)
                for o in range(H2 // P):
                    b = begin(s, "hidden2", o)
                    for k in range(H1 // P):
                        if o == 0:
                            copied(s, "hidden1", k)
                        last = nc.tensor.matmul(postP[:, b, :], w2_sb[:, k, o * P:(o + 1) * P], h1T[:, k, :],
                                                start=k == 0, stop=k == H1 // P - 1)
                    last.then_inc(post_full[b], 1)
                b = begin(s, "y", 0)
                for k in range(H2 // P):
                    copied(s, "hidden2", k)
                    last = nc.tensor.matmul(postP[0:1, b, :], w3_sb[:, k:k + 1], h2T[:, k, :],
                                            start=k == 0, stop=k == H2 // P - 1)
                last.then_inc(post_full[b], 1)

            def superblock(s, more):
                for h in range(2):
                    for kind, x, y in order(h, h == 0 or more):
                        if kind == "rows":
                            transpose_rows(s, x, y)
                        elif kind == "gram":
                            gram_unit(s, x, y)
                        else:
                            if y % 2 == 0:
                                if y + 2 < NHOT:
                                    spread_ids(s, h, y // 2 + 1)
                                elif h == 0:
                                    spread_ids(s, 1, 0)
                                elif more:
                                    spread_ids(s + 1, 0, 0)
                            if more and h == 0:
                                wait(lo_ready, y + 1)
                            pick_hot(s, h, y)
                tower(s)

            spread_ids(0, 0, 0)
            with pe.Fori(0, NSB - 1) as s:
                superblock(s, True)
            superblock(NSB - 1, False)


def kernel(**inputs):
    import concourse.bacc as _bacc
    from concourse import mybir as _mybir
    from concourse.bass_utils import run_bass_kernel_spmd as _run

    nc = _bacc.Bacc("TRN2", target_bir_lowering=False, num_devices=1)
    arrays = {}

    def dram(name, a):
        a = np.ascontiguousarray(a)
        arrays[name] = a
        return nc.dram_tensor(name, a.shape, _mybir.dt.from_np(a.dtype), kind="ExternalInput").ap()

    def columns(name):
        return np.asarray(inputs[name]).reshape(-1, P).T

    w1 = np.asarray(inputs["W_top1"])
    order = pair_rows() + list(range(NPAIR, w1.shape[0]))
    all_ids = np.asarray(inputs["ids"])
    hot_ids = all_ids[:, HOT].reshape(NSB, 2, HALF, NHOT).transpose(3, 1, 0, 2).reshape(2 * NHOT, NSB * HALF)
    bottom = dram("bottom", inputs["r_bottom_output"])
    ids = dram("ids", np.ascontiguousarray(all_ids[:, COLD]).view(np.uint32))
    hot = dram("hot_ids", hot_ids)
    tables = [dram(f"table_{t}", inputs[f"tbl_{t}"]) for t in range(TABLES)]
    w = [dram("w1", w1[order]), dram("b1", columns("b_top1")), dram("w2", inputs["W_top2"]),
         dram("b2", columns("b_top2")), dram("w3", columns("W_top3"))]
    out = nc.dram_tensor("y", (1, BATCH), _mybir.dt.float32, kind="ExternalOutput").ap()
    dlrm_tower(nc, bottom, ids, hot, tables, *w, out)
    r = _run(nc, [arrays], core_ids=[0])
    return r.results[0]["y"].reshape(BATCH, 1)
```

```python
import concourse.bass as bass
from concourse import mybir
from contextlib import ExitStack
import numpy as np

P = 128
BATCH = 2048
TABLES = 26
NF = TABLES + 1
TABLE_ROWS = [12500, 125000, 1250, 12500, 1250, 12500, 12500, 1250, 1250, 1000, 12500, 12500, 1250, 1250,
              12500, 1250, 12500, 1250, 1250, 1250, 1250, 1000, 1000, 1250, 1000, 1250]
HOT = [4, 2, 9, 21, 22, 24]
GATHERED_TOO = [0, 1]
COLD = [t for t in range(TABLES) if t not in HOT]
HP = 125
CUT = [TABLE_ROWS[t] // HP for t in HOT]
PARTS = 2
NHOT, NCOLD = len(HOT), len(COLD)
GATHERED = [COLD + HOT[:k] for k in GATHERED_TOO]
PICKED = [list(range(k, NHOT)) for k in GATHERED_TOO]
LOADED = PICKED[0] + [n for n in range(NHOT) if n not in PICKED[0]]
NPICKED = sum(len(p) for p in PICKED)
ORDER = [0] + [t + 1 for t in COLD] + [t + 1 for t in HOT]

ROWS = 4
SBLK = ROWS * P
HALF = SBLK // 2
NSB = BATCH // SBLK
Q = 4
GPR = P // Q
GU = 4
UNITS = GPR // GU
NJ = NF - 1
H1, H2 = 512, 256
SLOTS = [(m, i) for m in range(NJ // 2) for i in range(2 * m + 2)]
NSLOT = len(SLOTS)
REST = NSLOT - P
REST_AT = 64
MGROUPS = [list(range(m, min(m + 4, NJ // 2))) for m in range(0, NJ // 2, 4)]
GRAM_ROWS = (Q - 1) * 32 + NJ
W1_PARTS = 4
FGROUPS = [[list(range(f, min(f + 4, 1 + len(g)))) for f in range(0, 1 + len(g), 4)] for g in GATHERED]
MAX_ROWS = 1 + max(len(g) for g in GATHERED)


def w1_rows():
    row = {}
    for i in range(NF):
        for j in range(i + 1, NF):
            row[(i, j)] = len(row)
    of = [[row.get(tuple(sorted((ORDER[i], ORDER[2 * m + 1 + k]))), -1) for m, i in SLOTS] for k in range(2)]
    gap = [-1] * (REST_AT - REST)
    rest = of[0][P:] + gap + of[1][P:] + gap
    return [of[0][:P], of[1][:P], rest, [len(row) + d for d in range(P)]]


def dlrm_tower(nc, bottom, ids, hot_ids, tables, w1, b1, w2, b2, w3, out):
    F32 = mybir.dt.float32
    F32R = mybir.dt.float32r
    I32 = mybir.dt.int32
    U32 = mybir.dt.uint32
    ALU = mybir.AluOpType
    ACT = mybir.ActivationFunctionType

    with ExitStack() as ctx:
        def sb(name, shape, dt=F32):
            return ctx.enter_context(nc.sbuf_tensor(name, shape, dt))

        def psum(name, shape):
            return ctx.enter_context(nc.psum_tensor(name, shape, F32))

        def sem(name):
            return ctx.enter_context(nc.semaphore(name))

        idx_all = sb("idx_all", [P, NSB, ROWS, MAX_ROWS - 1], U32)
        idx_cur = sb("idx_cur", [P, ROWS, MAX_ROWS - 1], U32)
        rows = sb("rows", [P, ROWS, MAX_ROWS, P])
        hot_hi = [sb(f"hot_hi_{n}", [HP, CUT[n], P], F32R) for n in range(NHOT)]
        hot_lo = [sb(f"hot_lo_{n}", [HP, CUT[n], P], F32R) for n in range(NHOT)]
        hot_idf = sb("hot_idf", [P, NSB, HALF], F32R)
        onehot = sb("onehot", [HP, 2, PARTS, max(CUT) // PARTS, HALF], F32R)
        rowid = {c: sb(f"rowid_{c}", [HP, c]) for c in sorted(set(CUT))}
        embT = sb("embT", [P, 2, P, 32])
        botT = sb("botT", [P, 2, HALF])
        gram = sb("gram", [P, NJ, 2 * GPR])
        zrow = sb("zrow", [P, 2 * P, Q])
        zT = sb("zT", [P, 3, HALF])
        h1T = sb("h1T", [P, H1 // P, HALF])
        h2T = sb("h2T", [P, H2 // P, HALF])
        yrow = sb("yrow", [1, HALF])
        w1_sb = sb("w1_sb", [P, W1_PARTS, H1])
        w2_sb = sb("w2_sb", [P, H1 // P, H2])
        w3_sb = sb("w3_sb", [P, H2 // P])
        b1_sb = sb("b1_sb", [P, H1 // P])
        b2_sb = sb("b2_sb", [P, H2 // P])
        ident = sb("ident", [P, P])
        identR = sb("identR", [P, P], F32R)
        perm = sb("perm", [P, 32, Q])

        def beside(k):
            flat = rows[0:HP, 1 + k // 2, 1:, :].rearrange("p f d -> p (f d)")
            before = CUT[LOADED[k - 1]] * P if k % 2 else 0
            return flat[:, before:before + CUT[LOADED[k]] * P]

        staging = {n: beside(k) for k, n in enumerate(LOADED)}
        hot_int = w1_sb[0:2 * NHOT, 0:NSB * HALF // H1, :].rearrange("p c n -> p (c n)").bitcast(I32)

        featP = psum("featP", [P, 2, 4, P])
        gramP = psum("gramP", [P, 2, 512])
        idsP = psum("idsP", [P, 2, 2, HALF])
        postP = psum("postP", [P, 2, 512])

        ids_in = sem("ids_in")
        hot_ids_in = sem("hot_ids_in")
        table_in = [sem(f"table_in_{n}") for n in range(NHOT)]
        weights_in = sem("weights_in")
        hi_ready = sem("hi_ready")
        lo_ready = sem("lo_ready")
        ident_zero = sem("ident_zero")
        ident_ready = sem("ident_ready")
        rowid_ready = sem("rowid_ready")
        idf_zero = sem("idf_zero")
        consts_ready = sem("consts_ready")
        idx_ready = sem("idx_ready")
        gathers_begun = sem("gathers_begun")
        rows_in = [[sem(f"rows_in_{r}_{g}") for g in range(len(FGROUPS[r // 2]))] for r in range(ROWS)]
        bottom_in = [sem(f"bottom_in_{r}") for r in range(ROWS)]
        rows_used = [sem(f"rows_used_{r}") for r in range(ROWS)]
        onehot_ready = sem("onehot_ready")
        onehot_used = sem("onehot_used")
        ids_full = [sem(f"ids_full_{b}") for b in range(2)]
        feat_full = [sem(f"feat_full_{b}") for b in range(2)]
        feat_free = [sem(f"feat_free_{b}") for b in range(2)]
        gram_full = [sem(f"gram_full_{b}") for b in range(2)]
        gram_free = [sem(f"gram_free_{b}") for b in range(2)]
        post_full = [sem(f"post_full_{b}") for b in range(2)]
        post_free = [sem(f"post_free_{b}") for b in range(2)]
        y_stored = sem("y_stored")
        y_free = sem("y_free")

        bottom_t = bottom.rearrange("(t p) d -> t p d", p=P)
        NWEIGHTS = 5

        def start(h):
            hots = [("hot", h, n) for n in PICKED[h]]
            groups = [("rows", 2 * h, g) for g in range(len(FGROUPS[h]))]
            steps = hots[:2]
            for k in range(len(groups)):
                steps += groups[k:k + 1] + hots[k + 2:k + 3]
            return steps + hots[len(groups) + 2:]

        def matrices(h):
            groups = [("rows", 2 * h + 1, g) for g in range(len(FGROUPS[h]))]
            steps = []
            for u in range(UNITS):
                steps += [("gram", 2 * h, u)] + groups[u - 1:u] * (u > 0)
            steps += groups[UNITS - 1:]
            return steps + [("gram", 2 * h + 1, u) for u in range(UNITS)]

        def tower(h):
            return ([("pairs", h, c) for c in range(len(MGROUPS))] + [("pairsT", h, 0), ("pairsT", h, 1)]
                    + [("hidden1", h, 0), ("hidden1", h, 1), ("hidden2", h, 0), ("y", h, 0)])

        BEFORE = [1, 0, 1, 1, 1, 1, 1, 1, 2, len(start(1))]

        def half(s, h, more):
            fill = start(1 - h) if h == 0 or more else []
            steps = [(s, step) for step in matrices(h)]
            for before, step in zip(BEFORE, tower(h)):
                steps += [(s + h, f) for f in fill[:before]] + [(s, step)]
                fill = fill[before:]
            return steps + [(s + h, f) for f in fill]

        FEAT = [x for h in range(2) for x in start(h) + matrices(h) if x[0] != "gram"]
        HOT_OF = [[("hot", h, n) for n in PICKED[h]] for h in range(2)]
        GRAM = [("gram", r, u) for r in range(ROWS) for u in range(UNITS)]
        IDS = [(h, v) for h in range(2) for v in range((len(PICKED[h]) + 1) // 2)]
        POST = tower(0) + tower(1)
        VECTOR_STEPS = [(kind, h, c) for h in range(2) for kind, c in
                        (("pairs", 1), ("hidden1", 0), ("hidden2", 0))]

        def used(ring, s, item):
            u = ring.index(item)
            return u % 2, s * len(ring[u % 2::2]) + u // 2

        def hot_at(h, n):
            return h * len(PICKED[0]) + PICKED[h].index(n)

        block = ctx.enter_context(nc.Block())

        @block.sync
        def _(sp):
            sp.dma_start(idx_all[:], ids.rearrange("(s r p) f -> p s r f", p=P, r=ROWS)).then_inc(ids_in, 16)
            sp.dma_start(hot_int, hot_ids).then_inc(hot_ids_in, 16)
            for r in range(ROWS):
                sp.dma_start(rows[:, r, 0, :], bottom_t[r]).then_inc(bottom_in[r], 16)
            for n in LOADED:
                sp.dma_start(staging[n], tables[HOT[n]].rearrange("(p c) d -> p (c d)", p=HP)).then_inc(table_in[n], 16)
            sp.wait_ge(lo_ready, NHOT)
            sp.dma_start(w1_sb[:], w1.rearrange("(c p) n -> p c n", p=P)).then_inc(weights_in, 16)
            sp.dma_start(w2_sb[:], w2.rearrange("(c p) n -> p c n", p=P)).then_inc(weights_in, 16)
            for dst, src in ((w3_sb, w3), (b1_sb, b1), (b2_sb, b2)):
                sp.dma_start(dst[:], src).then_inc(weights_in, 16)

            def store(s, h):
                b, n = used(POST, s, ("y", h, 0))
                sp.wait_ge(post_free[b], n + 2)
                sp.dma_start(out[:, bass.ds(s * SBLK + h * HALF, HALF)], yrow[0:1, :]).then_inc(y_stored, 16)
                sp.wait_ge(y_stored, s * 32 + (16 * h + 16))
                sp.sem_inc(y_free, 1)

            sp.sem_inc(y_free, 1)
            with sp.Fori(0, NSB - 1) as s:
                for h in range(2):
                    for r in (2 * h, 2 * h + 1):
                        sp.wait_ge(rows_used[r], s + 2)
                        sp.dma_start(rows[:, r, 0, :],
                                     bottom_t[bass.ds((s + 1) * ROWS + r, 1), :, :].rearrange("t p d -> (t p) d")
                                     ).then_inc(bottom_in[r], 16)
                    store(s, h)
            for h in range(2):
                store(NSB - 1, h)
            sp.wait_ge(y_stored, 2 * 16 * NSB)

        @block.gpsimd
        def _(pool):
            nc.gpsimd.memset(ident[:], 0.0).then_inc(ident_zero, 1)
            pool.wait_ge(ident_zero, 1)
            nc.gpsimd.affine_select(out=ident[:], in_=ident[:], compare_op=ALU.not_equal, fill=1.0, base=0,
                                    pattern=[[-1, P]], channel_multiplier=1).then_inc(ident_ready, 1)
            for c in rowid:
                nc.gpsimd.iota(rowid[c][:], [[1, c]], base=0, channel_multiplier=c,
                               allow_small_or_imprecise_dtypes=True).then_inc(rowid_ready, 1)
            with pool.Fori(0, NSB) as s:
                for r in range(ROWS):
                    if r > 0:
                        pool.wait_ge(lo_ready, 2 * r)
                    pool.wait_ge(idx_ready, s * ROWS + (r + 1))
                    pool.sem_inc(gathers_begun, 1)
                    for k, t in enumerate(GATHERED[r // 2]):
                        nc.gpsimd.indirect_dma_start(
                            rows[:, r, k + 1, :], None, tables[t],
                            bass.IndirectOffsetOnAxis(ap=idx_cur[:, r, k:k + 1], axis=0),
                        ).then_inc(rows_in[r][(k + 1) // 4], 16)

        def copy(eng, dst, src):
            return nc.vector.tensor_copy(dst, src) if eng is nc.vector else nc.scalar.copy(dst, src)

        def copy_gram(eng, b, r, u, part):
            lo = r % 2 * GPR + GU * u
            for q in (2 * part, 2 * part + 1):
                end = min(32 * q + 32, GRAM_ROWS)
                last = copy(eng, gram[32 * q:end, :, lo:lo + GU],
                            gramP[32 * q:end, b, 0:GU * Q * NJ].rearrange(
                                "p (g c) -> p c g", g=GU)[:, q * NJ:(q + 1) * NJ, :])
            return last

        def copy_post(eng, b, kind, h, c):
            if kind == "pairs":
                for x, m in enumerate(MGROUPS[c]):
                    at, n = SLOTS.index((m, 0)), 2 * m + 2
                    op = copy(eng, zrow[:, at:at + n, :].rearrange("p n q -> p (n q)"),
                              postP[:, b, x * P:x * P + Q * n])
            elif kind == "pairsT":
                src = postP[:, b, :].rearrange("p (q k g) -> p k g q", q=Q, k=2)
                if c == 0:
                    op = copy(eng, zT[:, 0:2, :].rearrange("p k (g q) -> p k g q", q=Q), src)
                else:
                    dst = zT[:, 2, :].rearrange("p (g q) -> p g q", q=Q)
                    for k in range(2):
                        op = copy(eng, dst[REST_AT * k:REST_AT * (k + 1), :, :], src[0:REST_AT, k, :, :])
            elif kind == "y":
                op = copy(eng, yrow[0:1, :], postP[0:1, b, 0:HALF])
            else:
                for k in range(2):
                    o = 2 * c + k
                    dst = (h1T if kind == "hidden1" else h2T)[:, o, :]
                    bias = (b1_sb if kind == "hidden1" else b2_sb)[:, o:o + 1]
                    src = postP[:, b, k * HALF:(k + 1) * HALF]
                    if eng is nc.vector:
                        op = nc.vector.tensor_scalar(dst, src, bias, 0.0, ALU.add, ALU.max)
                    else:
                        op = nc.scalar.activation(dst, src, ACT.Relu, bias=bias)
            return op

        def on_vector(step):
            return step in VECTOR_STEPS

        def shared(r, u):
            return r % 2 == 1 or u >= UNITS // 2

        @block.vector
        def _(dve):
            nc.vector.memset(embT[:, :, :, NF:32], 0.0).then_inc(consts_ready, 1)
            nc.vector.memset(zrow[:, NSLOT:, :], 0.0).then_inc(consts_ready, 1)
            nc.vector.memset(gram[(Q - 1) * 32:P, :, :], 0.0).then_inc(consts_ready, 1)
            nc.vector.memset(hot_idf[:].bitcast(F32), 0.0).then_inc(idf_zero, 1)
            dve.wait_ge(ident_ready, 1)
            nc.vector.tensor_copy(perm[:], ident[:].rearrange("p (q i) -> p i q", q=Q)).then_inc(consts_ready, 1)
            nc.vector.tensor_copy(identR[:], ident[:]).then_inc(consts_ready, 1)
            dve.wait_ge(hot_ids_in, 16)
            dve.wait_ge(idf_zero, 1)
            nc.vector.tensor_copy(hot_idf[0:2 * NHOT, :, :].rearrange("p s b -> p (s b)"),
                                  hot_int).then_inc(consts_ready, 1)
            dve.wait_ge(rowid_ready, len(rowid))

            def split(k, n):
                dve.wait_ge(hi_ready, k + 1)
                nc.vector.tensor_tensor(hot_lo[n][:].rearrange("p c d -> p (c d)"), staging[n],
                                        hot_hi[n][:].bitcast(F32).rearrange("p c d -> p (c d)"),
                                        ALU.subtract).then_inc(lo_ready, 1)

            def make_onehot(s, h, n, first=False):
                at = PICKED[h].index(n)
                b, k = used(IDS, s, (h, at // 2))
                if at % 2 == 0:
                    dve.wait_ge(ids_full[b], k + 1)
                if at == 0 and not first:
                    fb, fk = used(FEAT, s, ("hot", 1 - h, NHOT - 1))
                    dve.wait_ge(feat_full[fb], fk + (1 if h == 1 else 1 - len(FEAT[fb::2])))
                m = CUT[n] // PARTS
                for k in range(PARTS):
                    if at >= 2:
                        if k < PARTS - 1:
                            dve.wait_ge(onehot_used, s * NPICKED + (hot_at(h, n - 2) + 1))
                        else:
                            fb, fk = used(FEAT, s, ("hot", h, n - 2))
                            dve.wait_ge(feat_full[fb], fk + 1)
                    nc.vector.tensor_tensor(
                        onehot[:, at % 2, k, 0:m, :],
                        idsP[0:HP, b, at % 2, :].unsqueeze(1).to_broadcast([HP, m, HALF]),
                        rowid[CUT[n]][:, k * m:(k + 1) * m].unsqueeze(2).to_broadcast([HP, m, HALF]),
                        ALU.is_equal).then_inc(onehot_ready, 1)

            def run(steps):
                for s, step in steps:
                    kind, h, n = step
                    if kind == "hot" and n + 2 in PICKED[h]:
                        make_onehot(s, h, n + 2)
                    elif kind == "gram" and shared(h, n):
                        b, k = used(GRAM, s, step)
                        dve.wait_ge(gram_full[b], k + 1)
                        copy_gram(nc.vector, b, h, n, 1).then_inc(gram_free[b], 1)
                    elif kind in ("pairs", "pairsT", "hidden1", "hidden2") and on_vector(step):
                        b, k = used(POST, s, step)
                        dve.wait_ge(post_full[b], k + 1)
                        if kind == "hidden1" or kind == "hidden2":
                            dve.wait_ge(weights_in, 16 * NWEIGHTS)
                        copy_post(nc.vector, b, *step).then_inc(post_free[b], 1)

            def superblock(s, more):
                for h in range(2):
                    if h == 0 or more:
                        for n in PICKED[1 - h][:2]:
                            make_onehot(s + h, 1 - h, n)
                    run(half(s, h, more))

            for b in range(2):
                dve.sem_inc(feat_free[b], 1)
                dve.sem_inc(gram_free[b], 2)
                dve.sem_inc(post_free[b], 1)
            for k, n in enumerate(LOADED):
                if n in PICKED[0]:
                    make_onehot(0, 0, n, first=True)
                split(k, n)
            with dve.Fori(0, NSB - 1) as s:
                superblock(s, True)
            superblock(NSB - 1, False)

        @block.scalar
        def _(act):
            def copy_indices(s, r):
                act.wait_ge(rows_used[r], s + 1)
                nc.scalar.copy(idx_cur[:, r, :], idx_all[:, bass.ds(s, 1), r, :].rearrange("p s f -> p (s f)")
                               ).then_inc(idx_ready, 1)

            act.wait_ge(ids_in, 16)
            for r in range(ROWS):
                copy_indices(0, r)
            for n in LOADED:
                act.wait_ge(table_in[n], 16)
                nc.scalar.copy(hot_hi[n][:].rearrange("p c d -> p (c d)"), staging[n]).then_inc(hi_ready, 1)

            def copy_hot(s, h, n):
                b, k = used(FEAT, s, ("hot", h, n))
                act.wait_ge(feat_full[b], k + 1)
                for tile in range(2):
                    last = nc.scalar.copy(embT[:, tile, :, 1 + NCOLD + n], featP[:, b, tile, :])
                last.then_inc(feat_free[b], 1)

            def copy_rows(s, r, g):
                b, k = used(FEAT, s, ("rows", r, g))
                act.wait_ge(feat_full[b], k + 1)
                feats = FGROUPS[r // 2][g]
                if g == 0:
                    nc.scalar.copy(botT[:, r // 2, r % 2 * P:(r % 2 + 1) * P], featP[:, b, 0, :])
                nc.scalar.copy(embT[:, r % 2, :, feats[0]:feats[-1] + 1],
                               featP[:, b, 0:len(feats), :].rearrange("p f b -> p b f")).then_inc(feat_free[b], 1)

            def run(steps, more=False):
                for s, step in steps:
                    kind, x, y = step
                    if kind == "hot":
                        copy_hot(s, x, y)
                    elif kind == "rows":
                        copy_rows(s, x, y)
                    elif kind == "gram":
                        b, k = used(GRAM, s, step)
                        act.wait_ge(gram_full[b], k + 1)
                        copy_gram(nc.scalar, b, x, y, 0).then_inc(gram_free[b], 1)
                        if not shared(x, y):
                            copy_gram(nc.scalar, b, x, y, 1).then_inc(gram_free[b], 1)
                        if more and y == 0:
                            copy_indices(s + 1, x)
                    elif not on_vector(step):
                        b, k = used(POST, s, step)
                        act.wait_ge(post_full[b], k + 1)
                        if kind == "y":
                            act.wait_ge(y_free, s * 2 + (x + 1))
                        elif kind in ("hidden1", "hidden2"):
                            act.wait_ge(weights_in, 16 * NWEIGHTS)
                        copy_post(nc.scalar, b, *step).then_inc(post_free[b], 1)

            def superblock(s, more):
                for h in range(2):
                    run(half(s, h, more), more)

            run([(0, step) for step in start(0)])
            with act.Fori(0, NSB - 1) as s:
                superblock(s, True)
            superblock(NSB - 1, False)

        @block.tensor
        def _(pe):
            for r in range(ROWS):
                pe.sem_inc(rows_used[r], 1)
            pe.wait_ge(ident_ready, 1)
            pe.wait_ge(consts_ready, 6)

            def spread_ids(s, h, v):
                b, k = used(IDS, s, (h, v))
                for at, n in enumerate(PICKED[h][2 * v:2 * v + 2]):
                    row = 2 * n + h
                    last = nc.tensor.matmul(idsP[:, b, at, :], identR[:, row:row + 1].to_broadcast([P, P]),
                                            hot_idf[:, bass.ds(s, 1), :].rearrange("p s b -> p (s b)"),
                                            start=True, stop=True)
                last.then_inc(ids_full[b], 1)

            def pick_hot(s, h, n, first=False):
                b, k = used(FEAT, s, ("hot", h, n))
                pe.wait_ge(feat_free[b], k + 1)
                if first or n not in PICKED[0]:
                    pe.wait_ge(lo_ready, LOADED.index(n) + 1)
                acc = featP[:, b, 0:2, :].rearrange("p t b -> p (t b)")
                m = CUT[n] // PARTS
                for k in range(PARTS):
                    pe.wait_ge(onehot_ready, s * (NPICKED * PARTS) + (hot_at(h, n) * PARTS + k + 1))
                    for c in range(m):
                        columns = onehot[:, PICKED[h].index(n) % 2, k, c, :]
                        begin, end = k == c == 0, k == PARTS - 1 and c == m - 1
                        nc.tensor.matmul(acc, hot_hi[n][:, k * m + c, :], columns, start=begin, stop=False)
                        lo = nc.tensor.matmul(acc, hot_lo[n][:, k * m + c, :], columns, start=False, stop=end)
                    if k < PARTS - 1:
                        lo.then_inc(onehot_used, 1)
                lo.then_inc(feat_full[b], 1)

            def transpose_rows(s, r, g):
                b, k = used(FEAT, s, ("rows", r, g))
                feats = FGROUPS[r // 2][g]
                if g == 0:
                    pe.wait_ge(bottom_in[r], (s + 1) * 16)
                pe.wait_ge(rows_in[r][g], (s + 1) * (16 * sum(1 for f in feats if f > 0)))
                pe.wait_ge(feat_free[b], k + 1)
                for m, f in enumerate(feats):
                    last = nc.tensor.transpose(featP[:, b, m, :], rows[:, r, f, :], ident[:])
                last.then_inc(feat_full[b], 1)

            def gram_unit(s, r, u):
                b, k = used(GRAM, s, ("gram", r, u))
                if u == 0:
                    for side in range(2):
                        its = [x for x in FEAT[side::2] if x in HOT_OF[r // 2] or x[:2] == ("rows", r)]
                        fb, fk = used(FEAT, s, its[-1])
                        pe.wait_ge(feat_free[fb], fk + 2)
                pe.wait_ge(gram_free[b], 2 * k + 2)
                for m in range(GU):
                    at = (GU * u + m) * Q
                    last = nc.tensor.matmul(gramP[0:GRAM_ROWS, b, m * Q * NJ:(m + 1) * Q * NJ],
                                            embT[:, r % 2, at:at + Q, :].rearrange("p b f -> p (b f)")[:, 0:GRAM_ROWS],
                                            embT[:, r % 2, at:at + Q, 1:NF], start=True, stop=True)
                    if u == m == 0:
                        last.then_inc(rows_used[r], 1)
                last.then_inc(gram_full[b], 1)

            def tower_step(s, kind, h, c):
                b, k = used(POST, s, (kind, h, c))

                def copied(*item):
                    b, k = used(POST, s, item)
                    pe.wait_ge(post_free[b], k + 2)

                if kind == "pairs" and c == 0:
                    for u in (UNITS - 2, UNITS - 1):
                        gb, gk = used(GRAM, s, ("gram", 2 * h + 1, u))
                        pe.wait_ge(gram_free[gb], 2 * gk + 4)
                pe.wait_ge(post_free[b], k + 1)
                if kind == "pairs":
                    for x, m in enumerate(MGROUPS[c]):
                        last = nc.tensor.transpose(postP[:, b, x * P:(x + 1) * P],
                                                   gram[:, 2 * m:2 * m + 2, :].rearrange("p j g -> p (j g)"),
                                                   perm[:].rearrange("p i q -> p (i q)"))
                elif kind == "pairsT":
                    if c == 0:
                        for x in (len(MGROUPS) - 2, len(MGROUPS) - 1):
                            copied("pairs", h, x)
                    for q in range(Q):
                        last = nc.tensor.transpose(postP[:, b, q * P:(q + 1) * P], zrow[:, c * P:(c + 1) * P, q],
                                                   ident[:])
                elif kind == "hidden1":
                    for k in range(2):
                        o = 2 * c + k
                        bank = postP[:, b, k * HALF:(k + 1) * HALF]
                        col = slice(o * P, (o + 1) * P)
                        if o == 0:
                            pe.wait_ge(weights_in, 16 * NWEIGHTS)
                        nc.tensor.matmul(bank, w1_sb[:, 3, col], botT[:, h, :], start=True, stop=False)
                        for part in range(3):
                            if o == 0 and part != 1:
                                copied("pairsT", h, part // 2)
                            last = nc.tensor.matmul(bank, w1_sb[:, part, col], zT[:, part, :],
                                                    start=False, stop=part == 2)
                elif kind == "hidden2":
                    for o in range(H2 // P):
                        for k in range(H1 // P):
                            if o == 0 and k % 2 == 0:
                                copied("hidden1", h, k // 2)
                            last = nc.tensor.matmul(postP[:, b, o * HALF:(o + 1) * HALF],
                                                    w2_sb[:, k, o * P:(o + 1) * P],
                                                    h1T[:, k, :], start=k == 0, stop=k == H1 // P - 1)
                else:
                    copied("hidden2", h, 0)
                    for k in range(H2 // P):
                        last = nc.tensor.matmul(postP[0:1, b, 0:HALF], w3_sb[:, k:k + 1], h2T[:, k, :],
                                                start=k == 0, stop=k == H2 // P - 1)
                last.then_inc(post_full[b], 1)

            def run(steps, first=False):
                for s, step in steps:
                    kind, x, y = step
                    if kind == "rows":
                        transpose_rows(s, x, y)
                    elif kind == "gram":
                        gram_unit(s, x, y)
                    elif kind == "hot":
                        pick_hot(s, x, y, first)
                        picked = PICKED[x].index(y)
                        if (x, picked // 2 + 2) in IDS and picked % 2 == 1:
                            spread_ids(s, x, picked // 2 + 2)
                    else:
                        tower_step(s, *step)

            def superblock(s, more):
                for h in range(2):
                    if h == 0 or more:
                        for v in range(2):
                            spread_ids(s + h, 1 - h, v)
                    run(half(s, h, more))

            for v in range(2):
                spread_ids(0, 0, v)
            run([(0, step) for step in start(0)], first=True)
            with pe.Fori(0, NSB - 1) as s:
                superblock(s, True)
            superblock(NSB - 1, False)


def kernel(**inputs):
    import concourse.bacc as _bacc
    from concourse import mybir as _mybir
    from concourse.bass_utils import run_bass_kernel_spmd as _run

    nc = _bacc.Bacc("TRN2", target_bir_lowering=False, num_devices=1)
    arrays = {}

    def dram(name, a):
        a = np.ascontiguousarray(a)
        arrays[name] = a
        return nc.dram_tensor(name, a.shape, _mybir.dt.from_np(a.dtype), kind="ExternalInput").ap()

    def columns(name):
        return np.asarray(inputs[name]).reshape(-1, P).T

    w1 = np.asarray(inputs["W_top1"])
    zero = np.zeros((1, H1), w1.dtype)
    w1 = np.concatenate([w1[r:r + 1] if r >= 0 else zero for part in w1_rows() for r in part])
    all_ids = np.asarray(inputs["ids"])
    hot_ids = all_ids[:, HOT].reshape(NSB, 2, HALF, NHOT).transpose(3, 1, 0, 2).reshape(2 * NHOT, NSB * HALF)
    bottom = dram("bottom", inputs["r_bottom_output"])
    ids = dram("ids", np.ascontiguousarray(all_ids[:, max(GATHERED, key=len)]).view(np.uint32))
    hot = dram("hot_ids", hot_ids)
    tables = [dram(f"table_{t}", inputs[f"tbl_{t}"]) for t in range(TABLES)]
    w = [dram("w1", w1), dram("b1", columns("b_top1")), dram("w2", inputs["W_top2"]),
         dram("b2", columns("b_top2")), dram("w3", columns("W_top3"))]
    out = nc.dram_tensor("y", (1, BATCH), _mybir.dt.float32, kind="ExternalOutput").ap()
    dlrm_tower(nc, bottom, ids, hot, tables, *w, out)
    r = _run(nc, [arrays], core_ids=[0])
    return r.results[0]["y"].reshape(BATCH, 1)
```
